# Optimizing a Trainium2 kernel written in Bass

```python
import numpy as np
import jax
import jax.numpy as jnp

def _softmax(x, axis=-1):
    return jax.nn.softmax(x, axis=axis)

def _gelu(x):
    return jax.nn.gelu(x, approximate=True)

def _silu(x):
    return jax.nn.silu(x)

def _sigmoid(x):
    return jax.nn.sigmoid(x)

def _layernorm(x, axis=-1, eps=1e-05):
    m = jnp.mean(x, axis=axis, keepdims=True)
    v = jnp.var(x, axis=axis, keepdims=True)
    return (x - m) / jnp.sqrt(v + eps)

def _scatter_add(tgt, idx, src, axis=0):
    return tgt.at[idx].add(src)

def _segment_sum(src, seg, n):
    return jax.ops.segment_sum(src, seg, n)
kernel_name = 'mk_lm_tower_d1_tok_ids512_r4_5c5a82'

def setup_inputs(seed: int=0):
    np.random.seed(seed)
    _w = jnp.asarray

    def _rec_inputs():
        import jax
        import jax.numpy as jnp
        _rk = jax.random.key(seed)
        x = jax.random.randint(jax.random.fold_in(_rk, 1), (16, 512), 0, 12564, jnp.int32)
        return x
    x = _rec_inputs()

    def _L0_tok_setup():
        import jax, jax.numpy as jnp
        import numpy as np
        VOCAB = 50257
        PROJ_DIM = 128
        B, S = (8, 1024)
        key = jax.random.key(seed)
        kx, kw = jax.random.split(key)
        x = jax.random.randint(kx, (B, S), 0, VOCAB)
        W = jax.random.normal(kw, (PROJ_DIM, VOCAB), dtype=jnp.float32) * 0.02
        return {'x': x, 'W': W}
    _L0_tok_all = _L0_tok_setup()
    _L0_tok_in = {k: v for k, v in _L0_tok_all.items() if k in ('W',)}
    del _L0_tok_all

    def _L0_attn_setup():
        import jax, jax.numpy as jnp
        import numpy as np
        SQRT_DK = np.sqrt(512.0).astype(np.float32)
        key = jax.random.key(seed)
        k1, k2, k3 = jax.random.split(key, 3)
        x = jax.random.normal(k1, (16, 512, 128), dtype=jnp.float32)
        W1 = jax.random.normal(k2, (128, 10), dtype=jnp.float32) * 0.05
        W2 = jax.random.normal(k3, (10, 128), dtype=jnp.float32) * 0.05
        return {'x': x, 'W1': W1, 'W2': W2}
    _L0_attn_all = _L0_attn_setup()
    _L0_attn_in = {k: v for k, v in _L0_attn_all.items() if k in ('W1', 'W2')}
    del _L0_attn_all

    def _L0_ffn_setup():
        import jax, jax.numpy as jnp
        import numpy as np
        D = 128
        H = 8
        K = 4
        HD = D // H

        def _ln(x, w, b, eps=1e-05):
            m = x.mean(-1, keepdims=True)
            v = ((x - m) ** 2).mean(-1, keepdims=True)
            return (x - m) / jnp.sqrt(v + eps) * w + b

        def _spatial_experts(xn, idx, in_w, in_b, out_w, out_b):
            W = in_w[idx]
            qkv = jnp.einsum('btd,bed->bte', xn, W) + in_b[idx][:, None, :]
            q, k, v = jnp.split(qkv, 3, axis=-1)
            B, T, _ = xn.shape
            q = q.reshape(B, T, H, HD) * HD ** (-0.5)
            k = k.reshape(B, T, H, HD)
            v = v.reshape(B, T, H, HD)
            att = jax.nn.softmax(jnp.einsum('bthd,bshd->bhts', q, k), axis=-1)
            o = jnp.einsum('bhts,bshd->bthd', att, v).reshape(B, T, D)
            return jnp.einsum('btd,bod->bto', o, out_w[idx]) + out_b[idx][:, None, :]

        def _temporal_experts(xt, idx, qw, qb, kw, kb, vw, vb, pw, pb):
            B, T, _ = xt.shape
            q = (jnp.einsum('btd,bod->bto', xt, qw[idx]) + qb[idx][:, None, :]).reshape(B, T, H, HD)
            k = (jnp.einsum('btd,bod->bto', xt, kw[idx]) + kb[idx][:, None, :]).reshape(B, T, H, HD)
            v = (jnp.einsum('btd,bod->bto', xt, vw[idx]) + vb[idx][:, None, :]).reshape(B, T, H, HD)
            logits = jnp.einsum('bthd,bshd->bhts', q, k) * HD ** (-0.5)
            causal = jnp.tril(jnp.ones((T, T), dtype=bool))
            logits = jnp.where(causal, logits, -jnp.inf)
            att = jax.nn.softmax(logits, axis=-1)
            o = jnp.einsum('bhts,bshd->bthd', att, v).reshape(B, T, D)
            o = jnp.einsum('btd,bod->bto', o, pw[idx]) + pb[idx][:, None, :]
            return xt + o

        def _cross_mha(q_in, kv_in, in_w, in_b, out_w, out_b):
            B, T, _ = q_in.shape
            S = kv_in.shape[1]
            Wq, Wk, Wv = (in_w[:D], in_w[D:2 * D], in_w[2 * D:])
            bq, bk, bv = (in_b[:D], in_b[D:2 * D], in_b[2 * D:])
            q = (q_in @ Wq.T + bq).reshape(B, T, H, HD) * HD ** (-0.5)
            k = (kv_in @ Wk.T + bk).reshape(B, S, H, HD)
            v = (kv_in @ Wv.T + bv).reshape(B, S, H, HD)
            att = jax.nn.softmax(jnp.einsum('bthd,bshd->bhts', q, k), axis=-1)
            o = jnp.einsum('bhts,bshd->bthd', att, v).reshape(B, T, D)
            return o @ out_w.T + out_b
        key = jax.random.key(seed)
        ks = iter(jax.random.split(key, 40))
        B, T = (64, 64)
        p = lambda *shape: jax.random.normal(next(ks), shape, dtype=jnp.float32) * 0.02
        inp = {'x': jax.random.normal(next(ks), (B, T, D), dtype=jnp.float32), 'router_w1': p(128, D), 'router_b1': jnp.zeros((128,), jnp.float32), 'router_w2': p(2 * K, 128), 'router_b2': jnp.zeros((2 * K,), jnp.float32), 'norm_s_w': jnp.ones((D,), jnp.float32), 'norm_s_b': jnp.zeros((D,), jnp.float32), 'norm_t_w': jnp.ones((D,), jnp.float32), 'norm_t_b': jnp.zeros((D,), jnp.float32), 'sp_in_w': p(K, 3 * D, D), 'sp_in_b': jnp.zeros((K, 3 * D), jnp.float32), 'sp_out_w': p(K, D, D), 'sp_out_b': jnp.zeros((K, D), jnp.float32), 'tq_w': p(K, D, D), 'tq_b': jnp.zeros((K, D), jnp.float32), 'tk_w': p(K, D, D), 'tk_b': jnp.zeros((K, D), jnp.float32), 'tv_w': p(K, D, D), 'tv_b': jnp.zeros((K, D), jnp.float32), 'tp_w': p(K, D, D), 'tp_b': jnp.zeros((K, D), jnp.float32), 'cross_in_w': p(3 * D, D), 'cross_in_b': jnp.zeros((3 * D,), jnp.float32), 'cross_out_w': p(D, D), 'cross_out_b': jnp.zeros((D,), jnp.float32), 'norm_mlp_w': jnp.ones((D,), jnp.float32), 'norm_mlp_b': jnp.zeros((D,), jnp.float32), 'mlp_w1': p(4 * D, D), 'mlp_b1': jnp.zeros((4 * D,), jnp.float32), 'mlp_w2': p(D, 4 * D), 'mlp_b2': jnp.zeros((D,), jnp.float32)}
        return inp
    _L0_ffn_all = _L0_ffn_setup()
    _L0_ffn_in = {k: v for k, v in _L0_ffn_all.items() if k in ('router_w1', 'router_b1', 'router_w2', 'router_b2', 'norm_s_w', 'norm_s_b', 'norm_t_w', 'norm_t_b', 'sp_in_w', 'sp_in_b', 'sp_out_w', 'sp_out_b', 'tq_w', 'tq_b', 'tk_w', 'tk_b', 'tv_w', 'tv_b', 'tp_w', 'tp_b', 'cross_in_w', 'cross_in_b', 'cross_out_w', 'cross_out_b', 'norm_mlp_w', 'norm_mlp_b', 'mlp_w1', 'mlp_b1', 'mlp_w2', 'mlp_b2')}
    del _L0_ffn_all
    return {'x': x, 'L0_tok_W': _L0_tok_in['W'], 'L0_attn_W1': _L0_attn_in['W1'], 'L0_attn_W2': _L0_attn_in['W2'], 'L0_ffn_router_w1': _L0_ffn_in['router_w1'], 'L0_ffn_router_b1': _L0_ffn_in['router_b1'], 'L0_ffn_router_w2': _L0_ffn_in['router_w2'], 'L0_ffn_router_b2': _L0_ffn_in['router_b2'], 'L0_ffn_norm_s_w': _L0_ffn_in['norm_s_w'], 'L0_ffn_norm_s_b': _L0_ffn_in['norm_s_b'], 'L0_ffn_norm_t_w': _L0_ffn_in['norm_t_w'], 'L0_ffn_norm_t_b': _L0_ffn_in['norm_t_b'], 'L0_ffn_sp_in_w': _L0_ffn_in['sp_in_w'], 'L0_ffn_sp_in_b': _L0_ffn_in['sp_in_b'], 'L0_ffn_sp_out_w': _L0_ffn_in['sp_out_w'], 'L0_ffn_sp_out_b': _L0_ffn_in['sp_out_b'], 'L0_ffn_tq_w': _L0_ffn_in['tq_w'], 'L0_ffn_tq_b': _L0_ffn_in['tq_b'], 'L0_ffn_tk_w': _L0_ffn_in['tk_w'], 'L0_ffn_tk_b': _L0_ffn_in['tk_b'], 'L0_ffn_tv_w': _L0_ffn_in['tv_w'], 'L0_ffn_tv_b': _L0_ffn_in['tv_b'], 'L0_ffn_tp_w': _L0_ffn_in['tp_w'], 'L0_ffn_tp_b': _L0_ffn_in['tp_b'], 'L0_ffn_cross_in_w': _L0_ffn_in['cross_in_w'], 'L0_ffn_cross_in_b': _L0_ffn_in['cross_in_b'], 'L0_ffn_cross_out_w': _L0_ffn_in['cross_out_w'], 'L0_ffn_cross_out_b': _L0_ffn_in['cross_out_b'], 'L0_ffn_norm_mlp_w': _L0_ffn_in['norm_mlp_w'], 'L0_ffn_norm_mlp_b': _L0_ffn_in['norm_mlp_b'], 'L0_ffn_mlp_w1': _L0_ffn_in['mlp_w1'], 'L0_ffn_mlp_b1': _L0_ffn_in['mlp_b1'], 'L0_ffn_mlp_w2': _L0_ffn_in['mlp_w2'], 'L0_ffn_mlp_b2': _L0_ffn_in['mlp_b2']}

def reference(x, L0_tok_W, L0_attn_W1, L0_attn_W2, L0_ffn_router_w1, L0_ffn_router_b1, L0_ffn_router_w2, L0_ffn_router_b2, L0_ffn_norm_s_w, L0_ffn_norm_s_b, L0_ffn_norm_t_w, L0_ffn_norm_t_b, L0_ffn_sp_in_w, L0_ffn_sp_in_b, L0_ffn_sp_out_w, L0_ffn_sp_out_b, L0_ffn_tq_w, L0_ffn_tq_b, L0_ffn_tk_w, L0_ffn_tk_b, L0_ffn_tv_w, L0_ffn_tv_b, L0_ffn_tp_w, L0_ffn_tp_b, L0_ffn_cross_in_w, L0_ffn_cross_in_b, L0_ffn_cross_out_w, L0_ffn_cross_out_b, L0_ffn_norm_mlp_w, L0_ffn_norm_mlp_b, L0_ffn_mlp_w1, L0_ffn_mlp_b1, L0_ffn_mlp_w2, L0_ffn_mlp_b2):
    import jax
    import jax.numpy as jnp

    def _L0_tok_ref(x, W):
        import jax, jax.numpy as jnp
        import numpy as np
        VOCAB = 50257
        PROJ_DIM = 128
        B, S = (8, 1024)
        return jnp.take(W.T, x, axis=0)

    def _L0_attn_ref(x, W1, W2):
        import jax, jax.numpy as jnp
        import numpy as np
        SQRT_DK = np.sqrt(512.0).astype(np.float32)
        B, A, D = x.shape
        left = jnp.einsum('bad,dr->bar', x, W1)
        right = jnp.einsum('rd,bcd->brc', W2, x)
        scores = jnp.einsum('bar,brc->bac', left, right)
        attn = jax.nn.softmax(scores / SQRT_DK, axis=-1)
        out = jnp.einsum('bac,bcd->bad', attn, x)
        return out

    def _L0_ffn_ref(x, router_w1, router_b1, router_w2, router_b2, norm_s_w, norm_s_b, norm_t_w, norm_t_b, sp_in_w, sp_in_b, sp_out_w, sp_out_b, tq_w, tq_b, tk_w, tk_b, tv_w, tv_b, tp_w, tp_b, cross_in_w, cross_in_b, cross_out_w, cross_out_b, norm_mlp_w, norm_mlp_b, mlp_w1, mlp_b1, mlp_w2, mlp_b2):
        import jax, jax.numpy as jnp
        import numpy as np
        D = 128
        H = 8
        K = 4
        HD = D // H

        def _ln(x, w, b, eps=1e-05):
            m = x.mean(-1, keepdims=True)
            v = ((x - m) ** 2).mean(-1, keepdims=True)
            return (x - m) / jnp.sqrt(v + eps) * w + b

        def _spatial_experts(xn, idx, in_w, in_b, out_w, out_b):
            W = in_w[idx]
            qkv = jnp.einsum('btd,bed->bte', xn, W) + in_b[idx][:, None, :]
            q, k, v = jnp.split(qkv, 3, axis=-1)
            B, T, _ = xn.shape
            q = q.reshape(B, T, H, HD) * HD ** (-0.5)
            k = k.reshape(B, T, H, HD)
            v = v.reshape(B, T, H, HD)
            att = jax.nn.softmax(jnp.einsum('bthd,bshd->bhts', q, k), axis=-1)
            o = jnp.einsum('bhts,bshd->bthd', att, v).reshape(B, T, D)
            return jnp.einsum('btd,bod->bto', o, out_w[idx]) + out_b[idx][:, None, :]

        def _temporal_experts(xt, idx, qw, qb, kw, kb, vw, vb, pw, pb):
            B, T, _ = xt.shape
            q = (jnp.einsum('btd,bod->bto', xt, qw[idx]) + qb[idx][:, None, :]).reshape(B, T, H, HD)
            k = (jnp.einsum('btd,bod->bto', xt, kw[idx]) + kb[idx][:, None, :]).reshape(B, T, H, HD)
            v = (jnp.einsum('btd,bod->bto', xt, vw[idx]) + vb[idx][:, None, :]).reshape(B, T, H, HD)
            logits = jnp.einsum('bthd,bshd->bhts', q, k) * HD ** (-0.5)
            causal = jnp.tril(jnp.ones((T, T), dtype=bool))
            logits = jnp.where(causal, logits, -jnp.inf)
            att = jax.nn.softmax(logits, axis=-1)
            o = jnp.einsum('bhts,bshd->bthd', att, v).reshape(B, T, D)
            o = jnp.einsum('btd,bod->bto', o, pw[idx]) + pb[idx][:, None, :]
            return xt + o

        def _cross_mha(q_in, kv_in, in_w, in_b, out_w, out_b):
            B, T, _ = q_in.shape
            S = kv_in.shape[1]
            Wq, Wk, Wv = (in_w[:D], in_w[D:2 * D], in_w[2 * D:])
            bq, bk, bv = (in_b[:D], in_b[D:2 * D], in_b[2 * D:])
            q = (q_in @ Wq.T + bq).reshape(B, T, H, HD) * HD ** (-0.5)
            k = (kv_in @ Wk.T + bk).reshape(B, S, H, HD)
            v = (kv_in @ Wv.T + bv).reshape(B, S, H, HD)
            att = jax.nn.softmax(jnp.einsum('bthd,bshd->bhts', q, k), axis=-1)
            o = jnp.einsum('bhts,bshd->bthd', att, v).reshape(B, T, D)
            return o @ out_w.T + out_b
        pooled = x.mean(axis=1)
        h = jax.nn.gelu(pooled @ router_w1.T + router_b1, approximate=False)
        route = jax.nn.softmax(h @ router_w2.T + router_b2, axis=-1)
        idx_s = jnp.argmax(route[:, :K], axis=-1)
        idx_t = jnp.argmax(route[:, K:], axis=-1)
        xn = _ln(x, norm_s_w, norm_s_b)
        spatial_out = _spatial_experts(xn, idx_s, sp_in_w, sp_in_b, sp_out_w, sp_out_b)
        xt = _ln(x, norm_t_w, norm_t_b)
        temporal_out = _temporal_experts(xt, idx_t, tq_w, tq_b, tk_w, tk_b, tv_w, tv_b, tp_w, tp_b)
        fused = _cross_mha(spatial_out, temporal_out, cross_in_w, cross_in_b, cross_out_w, cross_out_b)
        x = x + fused
        h2 = _ln(x, norm_mlp_w, norm_mlp_b)
        x = x + (jax.nn.gelu(h2 @ mlp_w1.T + mlp_b1, approximate=False) @ mlp_w2.T + mlp_b2)
        return x
    h = _L0_tok_ref(x, L0_tok_W)
    h = h + _L0_attn_ref(_layernorm(h, axis=-1), L0_attn_W1, L0_attn_W2)
    h = h + _L0_ffn_ref(_layernorm(h, axis=-1), L0_ffn_router_w1, L0_ffn_router_b1, L0_ffn_router_w2, L0_ffn_router_b2, L0_ffn_norm_s_w, L0_ffn_norm_s_b, L0_ffn_norm_t_w, L0_ffn_norm_t_b, L0_ffn_sp_in_w, L0_ffn_sp_in_b, L0_ffn_sp_out_w, L0_ffn_sp_out_b, L0_ffn_tq_w, L0_ffn_tq_b, L0_ffn_tk_w, L0_ffn_tk_b, L0_ffn_tv_w, L0_ffn_tv_b, L0_ffn_tp_w, L0_ffn_tp_b, L0_ffn_cross_in_w, L0_ffn_cross_in_b, L0_ffn_cross_out_w, L0_ffn_cross_out_b, L0_ffn_norm_mlp_w, L0_ffn_norm_mlp_b, L0_ffn_mlp_w1, L0_ffn_mlp_b1, L0_ffn_mlp_w2, L0_ffn_mlp_b2)
    return h

_drawn_inputs = setup_inputs


def setup_inputs(seed=0):
    import zlib

    import numpy as np

    out = dict(_drawn_inputs(seed))
    spreads = {'L0_ffn_router_b1': (0.0, 0.8),
     'L0_ffn_router_b2': (0.0, 2.0),
     'L0_ffn_norm_s_w': (1.0, 0.6),
     'L0_ffn_norm_s_b': (0.0, 2.0),
     'L0_ffn_norm_t_w': (1.0, 0.6),
     'L0_ffn_norm_t_b': (0.0, 0.8),
     'L0_ffn_sp_in_b': (0.0, 2.0),
     'L0_ffn_sp_out_b': (0.0, 2.0),
     'L0_ffn_tq_b': (0.0, 2.0),
     'L0_ffn_tk_b': (0.0, 2.0),
     'L0_ffn_tv_b': (0.0, 0.8),
     'L0_ffn_tp_b': (0.0, 0.8),
     'L0_ffn_cross_in_b': (0.0, 0.408),
     'L0_ffn_cross_out_b': (0.0, 0.1),
     'L0_ffn_norm_mlp_w': (1.0, 0.6),
     'L0_ffn_norm_mlp_b': (0.0, 0.8),
     'L0_ffn_mlp_b1': (0.0, 0.302),
     'L0_ffn_mlp_b2': (0.0, 0.1)}
    factors = {'L0_ffn_router_w1': 8.0,
     'L0_ffn_router_w2': 8.0,
     'L0_ffn_sp_in_w': 64.0,
     'L0_ffn_sp_out_w': 64.0,
     'L0_ffn_tq_w': 8.0,
     'L0_ffn_tk_w': 8.0,
     'L0_ffn_tv_w': 8.0,
     'L0_ffn_tp_w': 8.0}
    for name, (base, spread) in spreads.items():
        noise = np.random.default_rng([zlib.crc32(name.encode()), seed]).standard_normal(out[name].shape)
        drawn = base * np.exp(spread * noise) if base else spread * noise
        out[name] = jnp.asarray(drawn.astype(out[name].dtype))
    for name, factor in factors.items():
        out[name] = (out[name] * factor).astype(out[name].dtype)
    return out
```

```python
from contextlib import ExitStack

import concourse.bass as bass
from concourse import mybir

ALU = mybir.AluOpType
ACT = mybir.ActivationFunctionType
AX_X = mybir.AxisListType.X
F32 = mybir.dt.float32
BF16 = mybir.dt.bfloat16
I32 = mybir.dt.int32
U32 = mybir.dt.uint32

P = 128
B, T = 16, 512
NB = T // P
H, HD = 8, 16
K = 4
F = 4 * P
NPART = 3
Q_PARTS = (0, 0, 0, 1, 1, 2)
K_PARTS = (0, 1, 2, 0, 1, 0)
NPROD = len(Q_PARTS)
RA = NPROD * HD
RB = RA + NPART
GQ = H // 4
EPS = 1e-5
SCALE = HD ** -0.5
SCALE_D = 512.0 ** -0.5
NEG = -1e30
EXP_AND_LN = 6
LAG = 8
TILES = H * NB
RL, RC = 3, 3

W_Q, W_K, W_V, W_BQ, W_BK, W_BV = 0, P, 2 * P, 3 * P, 3 * P + 1, 3 * P + 2
IN_COLS = W_BV + P
O_W, O_B = 0, P
OUT_COLS = P + 1

DESK = (("mC", "qT", "kT", "vT", "oT"), ("mS", "qC", "kC", "vC", "oC"), ("mT", "qS", "kS", "vS", "oS"))
DESK_BATCH = {"mC": -2, "qT": 0, "kT": 0, "vT": 0, "oT": -1, "mS": 0, "qC": -1, "kC": -1, "vC": -1, "oC": -2,
              "mT": 0, "qS": 1, "kS": 1, "vS": 1, "oS": 0}
STEADY = (2, B - 1)
LAST = B + 2


def exists(b):
    return not isinstance(b, int) or 0 <= b < B


def desk_count(i):
    n = 3
    for j in range(i):
        n += sum(exists(j + DESK_BATCH[u]) for s in DESK for u in s)
    return n


DESK_FIRST = desk_count(STEADY[0])
DESK_USES = sum(len(s) for s in DESK)


def desk_use(name, b):
    if name[0] in "qkv" and name[1] == "S" and isinstance(b, int) and b == 0:
        return "qkv".index(name[0])
    i = b - DESK_BATCH[name]
    order = [u for s in DESK for u in s]
    at = order.index(name)
    if isinstance(i, int):
        return desk_count(i) + sum(exists(i + DESK_BATCH[u]) for u in order[:at])
    return DESK_FIRST + DESK_USES * (i - STEADY[0]) + at


def unit_no(kind, b):
    if kind == "C":
        return 3 * B - 1 if isinstance(b, int) and b == B - 1 else 3 * b + 4
    if isinstance(b, int) and b == 0:
        return "ST".index(kind)
    return 3 * b - 1 + "ST".index(kind)


def ring_place(kind, b, n, ring):
    steady = {"S": -1, "T": 0, "C": 4}
    u = unit_no(kind, b) if isinstance(b, int) else steady[kind] % 3
    assert 3 * TILES % ring == 0
    return (TILES * u + n) % ring


def at_least(eng, sem, value):
    if not isinstance(value, int) or value > 0:
        eng.wait_ge(sem, value)


def program(nc, x_ids, table, w12, router_w1, router_b1, router_w2, router_b2, norms, s_in, s_out, t_in, t_out,
            c_in, c_out, c_bias, mlp_w1, mlp_b1, mlp_w2, mlp_b2, out):
    out_v = out.rearrange("b (n p) d -> b p n d", p=P)
    with ExitStack() as ctx:
        ident = ctx.enter_context(nc.sbuf_tensor("ident", [P, P], F32))
        low = ctx.enter_context(nc.sbuf_tensor("low", [P, 1], F32))
        high = ctx.enter_context(nc.sbuf_tensor("high", [P, 1], F32))
        eps_t = ctx.enter_context(nc.sbuf_tensor("eps_t", [P, NB], F32))
        minus_half = ctx.enter_context(nc.sbuf_tensor("minus_half", [P, NB], F32))
        norm_cols = ctx.enter_context(nc.sbuf_tensor("norm_cols", [P, 6], F32))
        expert = ctx.enter_context(nc.sbuf_tensor("expert", [1, 2 * B], I32))
        X = ctx.enter_context(nc.sbuf_tensor("X", [P, B * NB, P + 2], F32))
        xhatT = ctx.enter_context(nc.sbuf_tensor("xhatT", [P, B, T], F32))
        psum = ctx.enter_context(nc.psum_tensor("psum", [P, 8, 512], F32))
        scrap = ctx.enter_context(nc.sbuf_tensor("scrap", [1, 1], F32))
        shared = (scrap, ident, low, high, eps_t, minus_half, norm_cols, expert, X, xhatT, psum)
        embed_and_mix(nc, shared, x_ids, table, w12, router_w1, router_b1, router_w2, router_b2, norms, out_v)
        attend(nc, shared, s_in, s_out, t_in, t_out, c_in, c_out, c_bias)
        feed_forward(nc, shared, mlp_w1, mlp_b1, mlp_w2, mlp_b2, out_v)


def settle(nc, scrap):
    nc.vector.memset(scrap[:], 0.0)


def tokens(tile, b, n):
    return tile[:, bass.ds(NB * b + n, 1), 0:P].rearrange("p o d -> p (o d)")


def embed_and_mix(nc, shared, x_ids, table, w12, router_w1, router_b1, router_w2, router_b2, norms, out_v):
    scrap, ident, low, high, eps_t, minus_half, norm_cols, expert, X, xhatT, psum = shared
    with ExitStack() as ctx:
        def sb(name, shape, dt=F32):
            return ctx.enter_context(nc.sbuf_tensor(name, shape, dt))

        def sem(name):
            return ctx.enter_context(nc.semaphore(name))

        ids = sb("ids", [P, B * NB], I32)
        w12_t = sb("w12_t", [P, 64])
        rw1 = sb("rw1", [P, P])
        rb1 = sb("rb1", [P, 1])
        rw2 = sb("rw2", [P, 2 * K])
        rb2 = sb("rb2", [B, 2 * K])
        place = sb("place", [B, K])
        mean_col = sb("mean_col", [P, 1])
        h = sb("h", [P, B * NB, P])
        six = sb("six", [P, NB, 6])
        mv = sb("mv", [P, NB, 2])
        vare = sb("vare", [P, NB])
        rstd = sb("rstd", [P, NB])
        xs = sb("xs", [P, NB, P])
        xh = sb("xh", [P, NB, P])
        xT = sb("xT", [P, T])
        lr_r = sb("lr_r", [64, T])
        parts = sb("parts", [64, NPART, B, T], BF16)
        qsd = sb("qsd", [P, B, T], BF16)
        ksd = sb("ksd", [P, B, T], BF16)
        mx = sb("mx", [P, B * NB])
        ng = sb("ng", [B * NB, P])
        ng_r = sb("ng_r", [B * NB, P])
        ng_p = sb("ng_p", [B * NB, NPART, P], BF16)
        probs = sb("probs", [P, NB, T])
        rsum = sb("rsum", [P, NB])
        pooled = sb("pooled", [P, B])
        rh = sb("rh", [P, B])
        rl = sb("rl", [B, 2 * K])
        rsc = sb("rsc", [B, 8])
        rex = sb("rex", [B, 2 * K])
        rpen = sb("rpen", [B, 2 * K])
        rid = sb("rid", [B, 2])
        rid_i = sb("rid_i", [B, 2], I32)
        lr = xhatT[0:64, :, :]

        loaded = sem("loaded")
        consts = sem("consts")
        halves = sem("halves")
        got = [sem("got0"), sem("got1")]
        six1, stats1, var1, rstd1 = sem("six1"), sem("stats1"), sem("var1"), sem("rstd1")
        normed1 = sem("normed1")
        x_kept = sem("x_kept")
        turned1 = sem("turned1")
        xT_ready = sem("xT_ready")
        lr_ready = sem("lr_ready")
        lr_f32, lr_hi, lr_rem, lr_mid, lr_lo = (sem(n) for n in ("lr_f32", "lr_hi", "lr_rem", "lr_mid", "lr_lo"))
        stacked = sem("stacked")
        scored = sem("scored")
        reduced = sem("reduced")
        max_turned = sem("max_turned")
        neg_step = sem("neg_step")
        rows_in = sem("rows_in")
        logits_in = sem("logits_in")
        exped = sem("exped")
        summed = sem("summed")
        recip = sem("recip")
        h2_ready = sem("h2_ready")
        h2_saved = sem("h2_saved")
        six2, stats2, var2, rstd2 = sem("six2"), sem("stats2"), sem("var2"), sem("rstd2")
        x_ready = sem("x_ready")
        x_stored = sem("x_stored")
        six3, stats3, var3, rstd3 = sem("six3"), sem("stats3"), sem("var3"), sem("rstd3")
        xh_ready = sem("xh_ready")
        turned2 = sem("turned2")
        xhatT_kept = sem("xhatT_kept")
        pooled_in = sem("pooled_in")
        r_pe, r_act, r_dve = sem("r_pe"), sem("r_act"), sem("r_dve")
        expert_in = sem("expert_in")
        TURN, LR, POOLED = 6, 5, 7
        LOADS = 7

        with nc.Block() as block:
            @block.sync
            def _(sp):
                sp.dma_start(ids[:], x_ids).then_inc(loaded, 16)
                sp.dma_start(w12_t[:], w12).then_inc(loaded, 16)
                sp.dma_start(rw1[:], router_w1).then_inc(loaded, 16)
                sp.dma_start(rb1[:], router_b1).then_inc(loaded, 16)
                sp.dma_start(rw2[:], router_w2).then_inc(loaded, 16)
                sp.dma_start(rb2[:], router_b2).then_inc(loaded, 16)
                sp.dma_start(norm_cols[:], norms).then_inc(loaded, 16)
                sp.wait_ge(lr_lo, B)
                for g in range(NPROD):
                    sp.dma_start(qsd[HD * g:HD * g + HD, :, :], parts[0:HD, Q_PARTS[g], :, :]).then_inc(stacked, 16)
                    sp.dma_start(ksd[HD * g:HD * g + HD, :, :],
                                 parts[32:32 + HD, K_PARTS[g], :, :]).then_inc(stacked, 16)
                sp.wait_ge(neg_step, 5)
                for k in range(NPART):
                    sp.dma_start(qsd[RA + k:RA + k + 1, :, :].rearrange("o b (n t) -> o (b n) t", t=P),
                                 ng_p[:, k, :]).then_inc(rows_in, 16)
                with sp.Fori(0, B) as b:
                    sp.wait_ge(h2_ready, b + 1)
                    sp.dma_start(out_v[bass.ds(b, 1), :, :, :].rearrange("b p n d -> p (b n) d"),
                                 h[:, bass.ds(NB * b, NB), :]).then_inc(h2_saved, 16)
                sp.wait_ge(r_dve, 10)
                sp.dma_start(expert[:], rid_i[:]).then_inc(expert_in, 16)
                sp.wait_ge(h2_saved, 16 * B)
                sp.wait_ge(expert_in, 16)

            @block.gpsimd
            def _(pool):
                nc.gpsimd.memset(ident[:], 0.0)
                nc.gpsimd.memset(mean_col[:], 1.0 / T)
                nc.gpsimd.memset(eps_t[:], EPS)
                nc.gpsimd.memset(minus_half[:], -0.5)
                nc.gpsimd.iota(place[:], pattern=[[1, K]], base=-K, channel_multiplier=0,
                               allow_small_or_imprecise_dtypes=True).then_inc(consts, 1)
                pool.wait_ge(consts, 1)
                nc.gpsimd.affine_select(out=ident[:], in_=ident[:], compare_op=ALU.not_equal, fill=1.0, base=0,
                                        pattern=[[-1, P]], channel_multiplier=1).then_inc(consts, 1)
                pool.wait_ge(loaded, 16 * LOADS)

                def fetch(b):
                    if b >= 2:
                        pool.wait_ge(got[b % 2], 64 * (b // 2))
                    for n in range(NB):
                        nc.gpsimd.indirect_dma_start(
                            h[:, NB * b + n, :], None, table,
                            bass.IndirectOffsetOnAxis(ap=ids[:, NB * b + n:NB * b + n + 1].bitcast(U32), axis=0),
                        ).then_inc(got[b % 2], 16)

                def root(b, stats, var, done):
                    pool.wait_ge(stats, b + 1)
                    nc.gpsimd.tensor_tensor(vare[:], mv[:, :, 1], eps_t[:], ALU.add).then_inc(var, 1)
                    pool.wait_ge(var, b + 1)
                    nc.gpsimd.tensor_tensor(rstd[:], vare[:], minus_half[:], ALU.pow).then_inc(done, 1)

                for b in range(B + 1):
                    if b < B:
                        fetch(b)
                    if b >= 1:
                        root(b - 1, stats1, var1, rstd1)
                with pool.Fori(0, B) as b:
                    root(b, stats2, var2, rstd2)
                    root(b, stats3, var3, rstd3)

            @block.vector
            def _(dve):
                def statistics(source, b, six_ready, stats):
                    for n in range(NB):
                        last = nc.vector.bn_stats(six[:, n, :], source(n))
                    last.then_inc(six_ready, 1)
                    dve.wait_ge(six_ready, b + 1)
                    settle(nc, scrap)
                    for n in range(NB):
                        last = nc.vector.bn_aggr(mv[:, n, :], six[:, n, :])
                    last.then_inc(stats, 1)

                def normalise(to, source, done):
                    for n in range(NB):
                        last = nc.vector.tensor_scalar(to[:, n, :], source(n), mv[:, n, 0:1], rstd[:, n:n + 1],
                                                       ALU.subtract, ALU.mult)
                    last.then_inc(done, 1)

                nc.vector.memset(X[:, :, P:P + 1], 1.0)
                nc.vector.memset(ksd[RA:RA + 32, :, :], 1.0)
                dve.wait_ge(consts, 2)
                nc.vector.tensor_reduce(high[:], ident[:].rearrange("p (j r) -> p j r", r=32)[:, :, HD:32],
                                        mybir.AxisListType.XY, ALU.add).then_inc(halves, 1)
                dve.wait_ge(halves, 1)
                nc.vector.tensor_scalar(low[:], high[:], -1.0, 1.0, ALU.mult, ALU.add)

                def first_norm(pair):
                    for odd in range(2):
                        b = 2 * pair + odd
                        dve.wait_ge(got[odd], 64 * pair + 64)
                        settle(nc, scrap)
                        statistics(lambda n: tokens(h, b, n), b, six1, stats1)
                        dve.wait_ge(rstd1, b + 1)
                        dve.wait_ge(stats1, b + 1)
                        at_least(dve, turned1, b)
                        normalise(xs, lambda n: tokens(h, b, n), normed1)
                        dve.wait_ge(normed1, b + 1)
                        nc.vector.tensor_copy(X[:, bass.ds(NB * b, NB), 0:P], xs[:]).then_inc(x_kept, 1)

                first_norm(0)
                with dve.Fori(1, B // 2) as pair:
                    first_norm(pair)

                with dve.Fori(0, B) as b:
                    dve.wait_ge(lr_hi, b + 1)
                    at = lr[:, bass.ds(b, 1), :]
                    nc.vector.tensor_tensor(at, at, parts[:, 0, bass.ds(b, 1), :], ALU.subtract).then_inc(lr_rem, 1)
                with dve.Fori(0, B) as b:
                    dve.wait_ge(lr_mid, b + 1)
                    nc.vector.tensor_tensor(parts[:, 2, bass.ds(b, 1), :], lr[:, bass.ds(b, 1), :],
                                            parts[:, 1, bass.ds(b, 1), :], ALU.subtract).then_inc(lr_lo, 1)

                with dve.Fori(0, B) as b:
                    dve.wait_ge(scored, b + 1)
                    nc.vector.tensor_reduce(mx[:, bass.ds(NB * b, NB)], psum[:, 0:4, :], AX_X, ALU.max)\
                        .then_inc(reduced, 1)
                dve.wait_ge(max_turned, 1)
                nc.vector.tensor_scalar(ng[:], psum[0:B * NB, 4, 0:P], -1.0, None, ALU.mult).then_inc(neg_step, 1)
                dve.wait_ge(neg_step, 1)
                nc.vector.tensor_copy(ng_p[:, 0, :], ng[:]).then_inc(neg_step, 1)
                dve.wait_ge(neg_step, 2)
                nc.vector.tensor_tensor(ng_r[:], ng[:], ng_p[:, 0, :], ALU.subtract).then_inc(neg_step, 1)
                dve.wait_ge(neg_step, 3)
                nc.vector.tensor_copy(ng_p[:, 1, :], ng_r[:]).then_inc(neg_step, 1)
                dve.wait_ge(neg_step, 4)
                nc.vector.tensor_tensor(ng_p[:, 2, :], ng_r[:], ng_p[:, 1, :], ALU.subtract).then_inc(neg_step, 1)

                def second_norms(b):
                    dve.wait_ge(summed, b + 1)
                    sums = psum[:, 4:6, :].rearrange("p a (c e) -> p a c e", c=2)
                    nc.vector.reciprocal(rsum[:].rearrange("p (a c) -> p a c", a=2), sums[:, :, :, P]).then_inc(recip, 1)
                    dve.wait_ge(recip, b + 1)
                    for n in range(NB):
                        last = nc.vector.scalar_tensor_tensor(
                            out=tokens(h, b, n), in0=sums[:, n // 2, n % 2, 0:P], scalar=rsum[:, n:n + 1],
                            in1=tokens(h, b, n), op0=ALU.mult, op1=ALU.add)
                    last.then_inc(h2_ready, 1)
                    dve.wait_ge(h2_ready, b + 1)
                    settle(nc, scrap)
                    statistics(lambda n: tokens(h, b, n), b, six2, stats2)
                    dve.wait_ge(rstd2, b + 1)
                    dve.wait_ge(stats2, b + 1)
                    at_least(dve, pooled_in, b)
                    at_least(dve, x_stored, b)
                    normalise(xs, lambda n: tokens(h, b, n), x_ready)
                    dve.wait_ge(x_ready, b + 1)
                    settle(nc, scrap)
                    statistics(lambda n: xs[:, n, :], b, six3, stats3)
                    dve.wait_ge(rstd3, b + 1)
                    dve.wait_ge(stats3, b + 1)
                    at_least(dve, turned2, b)
                    normalise(xh, lambda n: xs[:, n, :], xh_ready)

                second_norms(0)
                with dve.Fori(1, B) as b:
                    second_norms(b)

                dve.wait_ge(pooled_in, B)
                nc.vector.tensor_copy(pooled[:], psum[:, POOLED, 0:B]).then_inc(r_dve, 1)
                dve.wait_ge(r_pe, 2)
                nc.vector.tensor_tensor(rl[:], psum[0:B, 1, 0:2 * K], rb2[:], ALU.add).then_inc(r_dve, 1)
                dve.wait_ge(r_dve, 2)
                nc.vector.tensor_reduce(rsc[:, 0:1], rl[:], AX_X, ALU.max).then_inc(r_dve, 1)
                dve.wait_ge(r_dve, 3)
                nc.vector.tensor_scalar(rsc[:, 1:2], rsc[:, 0:1], -1.0, None, ALU.mult).then_inc(r_dve, 1)
                dve.wait_ge(r_act, 2)
                nc.vector.reciprocal(rsc[:, 3:4], rsc[:, 2:3]).then_inc(r_dve, 1)
                dve.wait_ge(r_dve, 5)
                nc.vector.tensor_scalar(rl[:], rex[:], rsc[:, 3:4], None, ALU.mult).then_inc(r_dve, 1)
                dve.wait_ge(r_dve, 6)
                nc.vector.tensor_reduce(rsc[:, 4:6], rl[:].rearrange("b (a k) -> b a k", a=2), AX_X, ALU.max)\
                    .then_inc(r_dve, 1)
                dve.wait_ge(r_dve, 7)
                for a in range(2):
                    last = nc.vector.scalar_tensor_tensor(out=rpen[:, K * a:K * a + K], in0=rl[:, K * a:K * a + K],
                                                          scalar=rsc[:, 4 + a:5 + a], in1=place[:],
                                                          op0=ALU.is_ge, op1=ALU.mult)
                last.then_inc(r_dve, 1)
                dve.wait_ge(r_dve, 8)
                nc.vector.tensor_reduce(rid[:], rpen[:].rearrange("b (a k) -> b a k", a=2), AX_X, ALU.min)\
                    .then_inc(r_dve, 1)
                dve.wait_ge(r_dve, 9)
                nc.vector.tensor_scalar(rid_i[:], rid[:], float(K), float(K - 1), ALU.add, ALU.min).then_inc(r_dve, 1)

            @block.scalar
            def _(act):
                def factors(b):
                    act.wait_ge(turned1, b + 1)
                    at_least(act, lr_ready, b)
                    nc.scalar.activation(xT[:], psum[:, TURN, :], ACT.Copy).then_inc(xT_ready, 1)
                    act.wait_ge(lr_ready, b + 1)
                    nc.scalar.activation(lr[:, bass.ds(b, 1), :].rearrange("p o t -> p (o t)"), psum[0:64, LR, :],
                                         ACT.Copy).then_inc(lr_f32, 1)

                factors(0)
                with act.Fori(1, B) as b:
                    factors(b)
                with act.Fori(0, B) as b:
                    act.wait_ge(lr_f32, b + 1)
                    nc.scalar.activation(parts[:, 0, bass.ds(b, 1), :], lr[:, bass.ds(b, 1), :], ACT.Copy)\
                        .then_inc(lr_hi, 1)
                with act.Fori(0, B) as b:
                    act.wait_ge(lr_rem, b + 1)
                    nc.scalar.activation(parts[:, 1, bass.ds(b, 1), :], lr[:, bass.ds(b, 1), :], ACT.Copy)\
                        .then_inc(lr_mid, 1)

                def soften(b):
                    act.wait_ge(logits_in, b + 1)
                    at_least(act, summed, b)
                    nc.scalar.activation(probs[:], psum[:, 0:4, :], ACT.Exp, scale=SCALE_D).then_inc(exped, 1)

                def keep(b):
                    act.wait_ge(x_ready, b + 1)
                    act.wait_ge(summed, b + 1)
                    nc.scalar.activation(X[:, bass.ds(NB * b, NB), 0:P], xs[:], ACT.Copy).then_inc(x_stored, 1)
                    act.wait_ge(turned2, b + 1)
                    nc.scalar.activation(xhatT[:, bass.ds(b, 1), :].rearrange("p o t -> p (o t)"),
                                         psum[:, TURN, :], ACT.Copy).then_inc(xhatT_kept, 1)

                soften(0)
                with act.Fori(1, B) as b:
                    soften(b)
                    keep(b - 1)
                keep(B - 1)
                act.wait_ge(r_pe, 1)
                nc.scalar.activation(rh[:], psum[:, 0, 0:B], ACT.Gelu, bias=rb1[:]).then_inc(r_act, 1)
                act.wait_ge(r_dve, 4)
                nc.scalar.activation(rex[:], rl[:], ACT.Exp, bias=rsc[:, 1:2], accum_out=rsc[:, 2:3]).then_inc(r_act, 1)

            @block.tensor
            def _(pe):
                pe.wait_ge(consts, 2)
                pe.wait_ge(loaded, 16 * LOADS)
                def factors(b):
                    pe.wait_ge(normed1, b + 1)
                    at_least(pe, xT_ready, b)
                    for n in range(NB):
                        last = nc.tensor.transpose(psum[:, TURN, P * n:P * n + P], xs[:, n, :], ident[:])
                    last.then_inc(turned1, 1)
                    pe.wait_ge(xT_ready, b + 1)
                    at_least(pe, lr_f32, b)
                    nc.tensor.matmul(psum[0:64, LR, :], w12_t[:], xT[:], start=True, stop=True).then_inc(lr_ready, 1)

                factors(0)
                with pe.Fori(1, B) as b:
                    factors(b)
                pe.wait_ge(stacked, 16 * 2 * NPROD)

                def scores(b):
                    at_least(pe, reduced, b)
                    for n in range(NB):
                        last = nc.tensor.matmul(
                            psum[:, n, :], qsd[0:RA, bass.ds(b, 1), P * n:P * n + P].rearrange("p o t -> p (o t)"),
                            ksd[0:RA, bass.ds(b, 1), :].rearrange("p o t -> p (o t)"), start=True, stop=True)
                    last.then_inc(scored, 1)

                scores(0)
                with pe.Fori(1, B) as b:
                    scores(b)
                pe.wait_ge(reduced, B)
                nc.tensor.transpose(psum[0:B * NB, 4, 0:P], mx[:], ident[:]).then_inc(max_turned, 1)
                pe.wait_ge(rows_in, 16 * NPART)
                pe.wait_ge(neg_step, 1)
                pe.wait_ge(x_kept, B)

                def mix(b):
                    at_least(pe, exped, b)
                    for n in range(NB):
                        last = nc.tensor.matmul(
                            psum[:, n, :], ksd[0:RB, bass.ds(b, 1), P * n:P * n + P].rearrange("p o t -> p (o t)"),
                            qsd[0:RB, bass.ds(b, 1), :].rearrange("p o t -> p (o t)"), start=True, stop=True)
                    last.then_inc(logits_in, 1)
                    pe.wait_ge(exped, b + 1)
                    at_least(pe, h2_ready, b)
                    for n in range(NB):
                        for s in range(NB):
                            last = nc.tensor.matmul(
                                psum[:, 4 + n // 2, 256 * (n % 2):256 * (n % 2) + P + 1],
                                probs[:, s, P * n:P * n + P],
                                X[:, bass.ds(NB * b + s, 1), 0:P + 1].rearrange("p o d -> p (o d)"),
                                start=(s == 0), stop=(s == NB - 1))
                    last.then_inc(summed, 1)

                def turn(b):
                    pe.wait_ge(x_ready, b + 1)
                    for n in range(NB):
                        last = nc.tensor.matmul(psum[:, POOLED, bass.ds(b, 1)], xs[:, n, :], mean_col[:],
                                                start=(n == 0), stop=(n == NB - 1))
                    last.then_inc(pooled_in, 1)
                    pe.wait_ge(xh_ready, b + 1)
                    at_least(pe, xhatT_kept, b)
                    for n in range(NB):
                        last = nc.tensor.transpose(psum[:, TURN, P * n:P * n + P], xh[:, n, :], ident[:])
                    last.then_inc(turned2, 1)

                mix(0)
                with pe.Fori(1, B) as b:
                    mix(b)
                    turn(b - 1)
                turn(B - 1)
                pe.wait_ge(r_dve, 1)
                pe.wait_ge(exped, B)
                nc.tensor.matmul(psum[:, 0, 0:B], rw1[:], pooled[:], start=True, stop=True).then_inc(r_pe, 1)
                pe.wait_ge(r_act, 1)
                nc.tensor.matmul(psum[0:B, 1, 0:2 * K], rh[:], rw2[:], start=True, stop=True).then_inc(r_pe, 1)


def attend(nc, shared, s_in, s_out, t_in, t_out, c_in, c_out, c_bias):
    scrap, ident, low, high, eps_t, minus_half, norm_cols, expert, X, xhatT, psum = shared
    with ExitStack() as ctx:
        def sb(name, shape, dt=F32):
            return ctx.enter_context(nc.sbuf_tensor(name, shape, dt))

        def sem(name):
            return ctx.enter_context(nc.semaphore(name))

        KINDS = "STC"
        ident_bf = sb("ident_bf", [P, P], BF16)
        mask_row = sb("mask_row", [P, P], BF16)
        mask_col = sb("mask_col", [P, P], BF16)
        w_in = {k: sb(f"w_in_{k}", [P, IN_COLS]) for k in KINDS}
        w_out = {k: sb(f"w_out_{k}", [P, OUT_COLS]) for k in KINDS}
        ob = sb("ob", [P, P])
        qs = {k: sb(f"qs_{k}", [P, H, T], BF16) for k in KINDS}
        ks = {k: sb(f"ks_{k}", [P, H, T], BF16) for k in KINDS}
        va = {k: sb(f"va_{k}", [P, NB, GQ, 4, 32]) for k in KINDS}
        mx = {k: sb(f"mx_{k}", [P, TILES]) for k in KINDS}
        xn = sb("xn", [P, T])
        xt = sb("xt", [P, T])
        scaled = sb("scaled", [P, T])
        xres = sb("xres", [P, T])
        s_outT = sb("s_outT", [P, T])
        t_outT = sb("t_outT", [P, T])
        f32 = [sb(f"f32_{c}", [P, T]) for c in "qk"]
        rem = [sb(f"rem_{c}", [P, T]) for c in "qk"]
        parts = [sb(f"parts_{c}", [P, NPART, T], BF16) for c in "qk"]
        ng = sb("ng2", [TILES, P])
        ng_r = sb("ng2_r", [TILES, P])
        ng_p = sb("ng2_p", [TILES, NPART, P], BF16)
        probs = sb("probs2", [P, 2, 4, T])
        u_low = sb("u_low", [P, T])
        s_low = sb("s_low", [P, T])
        u_all = sb("u_all", [P, T])
        s_all = sb("s_all", [P, T])
        s_right = sb("s_right", [P, T])
        s_log = sb("s_log", [P, T])
        s_recip = sb("s_recip", [P, T])
        oT = sb("oT", [P, T])

        consts = sem("consts2")
        ones_in = sem("ones_in")
        w_fixed = sem("w_fixed")
        win_in = {k: sem(f"win_in_{k}") for k in "ST"}
        wout_in = {k: sem(f"wout_in_{k}") for k in "ST"}
        scaled_in = sem("scaled_in")
        affine_done = sem("affine_done")
        desk_full = sem("desk_full")
        desk_free = sem("desk_free")
        f32_done, hi_done, rem_done, mid_done, lo_done = (
            sem(n) for n in ("f32_done", "hi_done", "rem_done", "mid_done", "lo_done"))
        v_ready = {k: sem(f"v_ready_{k}") for k in KINDS}
        stack_in = {k: sem(f"stack_in_{k}") for k in KINDS}
        rows_in = {k: sem(f"rows_in_{k}") for k in KINDS}
        scored = sem("scored2")
        reduced = sem("reduced2")
        neg_step = sem("neg_step2")
        logits_in = sem("logits_in2")
        exped = sem("exped2")
        summed = sem("summed2")
        low_out = sem("low_out")
        high_out = sem("high_out")
        swapped = sem("swapped")
        logged = sem("logged")
        recip = sem("recip2")
        o_ready = sem("o_ready")
        x_biased = sem("x_biased")

        LOGITS, SUMS, DESK_BANK = RL, RL + RC, RL + RC + 1
        desk = psum[:, DESK_BANK, :]
        sums = psum[:, SUMS, :]

        def affine_no(i, slot):
            if isinstance(i, int) and i == B:
                return 3 * (B - 1) + 2
            return 3 * i + 1 + slot if not isinstance(i, int) or i else 1 + slot

        def input_no(name, b):
            if name == "xres":
                return affine_no(b + 1, 0)
            if isinstance(b, int) and b == 0:
                return ("xn", "xt").index(name)
            return affine_no(b - 1, 1 + ("xn", "xt").index(name))

        def units(i, slot):
            return ((("T", i), ("S", i), ("C", i - 2), ("T", i - 1)),
                    (("C", i - 1), ("T", i), ("S", i), ("C", i - 2)),
                    (("S", i + 1), ("C", i - 1), ("T", i), ("S", i)))[slot]

        def before(kind, b):
            if kind == "T":
                return "S", b
            if kind == "C":
                return ("C", b - 1) if isinstance(b, int) and b == B - 1 else ("T", b + 1)
            if isinstance(b, int) and b < 2:
                return ("T", 0) if b else None
            return "C", b - 2

        def first_key(kind, tile):
            return P * (tile // 4 % NB) if kind == "T" else 0

        def whole_loop(eng, slot_program):
            for i in range(STEADY[0]):
                for slot in range(3):
                    slot_program(i, slot)
            nc.disable_value_cache = True
            with eng.Fori(STEADY[0], STEADY[1]) as i:
                for slot in range(3):
                    slot_program(i, slot)
            nc.disable_value_cache = False
            for i in range(STEADY[1], LAST):
                for slot in range(3):
                    slot_program(i, slot)

        with nc.Block() as block:
            @block.sync
            def _(sp):
                for tile, source in ((w_in["C"], c_in), (w_out["C"], c_out), (ob, c_bias)):
                    sp.dma_start(tile[:], source).then_inc(w_fixed, 16)

                def weights(kind, b, tile, packs, done, use):
                    if isinstance(b, int) and b >= B:
                        return
                    if not isinstance(b, int) or b >= 1:
                        sp.wait_ge(desk_free, desk_use(use, b - 1) + 1)
                    e = sp.value_load(expert[0:1, bass.ds(2 * b + "ST".index(kind), 1)], min_val=0, max_val=K - 1)
                    sp.dma_start(tile[:], packs[bass.ds(e, 1), :, :].rearrange("o p n -> p (o n)")).then_inc(done, 16)

                def stack(kind, b):
                    if exists(b):
                        if not isinstance(b, int) or b >= 1:
                            sp.wait_ge(logits_in, TILES * (unit_no(kind, b - 1) + 1))
                        for c, (tile, order) in enumerate(((qs[kind], Q_PARTS), (ks[kind], K_PARTS))):
                            sp.wait_ge(lo_done, 2 * unit_no(kind, b) + c + 1)
                            sp.wait_ge(mid_done, 2 * unit_no(kind, b) + c + 1)
                            for g in range(NPROD):
                                sp.dma_start(tile[HD * g:HD * g + HD, :, :],
                                             parts[c][:, order[g], :]).then_inc(stack_in[kind], 16)

                def slot_program(i, slot):
                    (kn, bn), _, (kb, bb), _ = units(i, slot)
                    if exists(bb):
                        sp.wait_ge(neg_step, 5 * (unit_no(kb, bb) + 1))
                        for k in range(NPART):
                            sp.dma_start(qs[kb][RA + k:RA + k + 1, :, :].rearrange("o h (n t) -> o (h n) t", t=P),
                                         ng_p[:, k, :]).then_inc(rows_in[kb], 16)
                    if slot == 0:
                        weights("S", i + 1, w_in["S"], s_in, win_in["S"], "vS")
                    if slot == 1:
                        weights("T", i + 1, w_in["T"], t_in, win_in["T"], "vT")
                        weights("S", i, w_out["S"], s_out, wout_in["S"], "oS")
                        weights("T", i, w_out["T"], t_out, wout_in["T"], "oT")
                    stack(kn, bn)

                weights("S", 0, w_in["S"], s_in, win_in["S"], "vS")
                weights("T", 0, w_in["T"], t_in, win_in["T"], "vT")
                stack("S", 0)
                whole_loop(sp, slot_program)

            @block.gpsimd
            def _(pool):
                nc.gpsimd.memset(mask_row[:], 0.0)
                nc.gpsimd.memset(mask_col[:], 0.0)
                for k in KINDS:
                    last = nc.gpsimd.memset(va[k][:], 1.0)
                last.then_inc(ones_in, 1)
                pool.wait_ge(ones_in, 1)
                nc.gpsimd.affine_select(out=mask_row[:], in_=mask_row[:], compare_op=ALU.is_ge, fill=NEG, base=0,
                                        pattern=[[-1, P]], channel_multiplier=1).then_inc(consts, 1)
                nc.gpsimd.affine_select(out=mask_col[:], in_=mask_col[:], compare_op=ALU.is_ge, fill=NEG, base=0,
                                        pattern=[[1, P]], channel_multiplier=-1).then_inc(consts, 1)

                def affine(to, b, norm, name):
                    number = input_no(name, b)
                    at_least(pool, affine_done, number)
                    w, s = (norm_cols[:, c:c + 1].broadcast_to([P, T]) for c in (2 * norm, 2 * norm + 1))
                    nc.gpsimd.tensor_tensor(scaled[:], xhatT[:, bass.ds(b, 1), :].rearrange("p o t -> p (o t)"), w,
                                            ALU.mult).then_inc(scaled_in, 1)
                    pool.wait_ge(scaled_in, number + 1)
                    nc.gpsimd.tensor_tensor(to[:], scaled[:], s, ALU.add).then_inc(affine_done, 1)

                def split(kind, b):
                    if not exists(b):
                        return
                    for c in range(2):
                        n = 2 * unit_no(kind, b) + c
                        pool.wait_ge(hi_done, n + 1)
                        at_least(pool, mid_done, n - 1)
                        nc.gpsimd.tensor_tensor(rem[c][:], f32[c][:], parts[c][:, 0, :], ALU.subtract)\
                            .then_inc(rem_done, 1)
                        pool.wait_ge(mid_done, n + 1)
                        nc.gpsimd.tensor_tensor(parts[c][:, 2, :], rem[c][:], parts[c][:, 1, :], ALU.subtract)\
                            .then_inc(lo_done, 1)

                def slot_program(i, slot):
                    (kn, bn), _, _, (ko, bo) = units(i, slot)
                    split(kn, bn)
                    if slot == 0 and exists(i - 1):
                        if not isinstance(i, int) or i >= 2:
                            pool.wait_ge(desk_free, desk_use("oT", i - 2) + 1)
                        affine(xres, i - 1, 1, "xres")
                    if slot == 1 and exists(i - 2):
                        xb = X[:, bass.ds(NB * (i - 2), NB), 0:P]
                        nc.gpsimd.tensor_tensor(xb, xb, ob[:].unsqueeze(1).broadcast_to([P, NB, P]), ALU.add)\
                            .then_inc(x_biased, 1)
                    if exists(bo):
                        u = unit_no(ko, bo)
                        pool.wait_ge(recip, u + 1)
                        at_least(pool, desk_full, (desk_use("o" + before(ko, bo)[0], before(ko, bo)[1]) + 1)
                                 if before(ko, bo) else 0)
                        nc.gpsimd.tensor_tensor(oT[:], u_all[:], s_recip[:], ALU.mult).then_inc(o_ready, 1)
                    if slot == 1 and exists(i + 1):
                        pool.wait_ge(desk_full, desk_use("vS", i) + 1)
                        affine(xn, i + 1, 0, "xn")
                    if slot == 2 and exists(i + 1):
                        pool.wait_ge(desk_full, desk_use("vT", i) + 1)
                        affine(xt, i + 1, 1, "xt")

                affine(xn, 0, 0, "xn")
                affine(xt, 0, 1, "xt")
                split("S", 0)
                pool.wait_ge(w_fixed, 48)
                whole_loop(pool, slot_program)

            @block.vector
            def _(dve):
                for k in KINDS:
                    nc.vector.memset(ks[k][RA:P, :, :], 1.0)
                nc.vector.tensor_copy(ident_bf[:], ident[:]).then_inc(consts, 1)
                dve.wait_ge(ones_in, 1)

                def reduce(kind, b, n):
                    u = unit_no(kind, b)
                    dve.wait_ge(scored, TILES * u + n + 1)
                    last_key = P * (n % NB + 1) if kind == "T" else T
                    nc.vector.tensor_reduce(mx[kind][:, n:n + 1], psum[:, ring_place(kind, b, n, RL), 0:last_key], AX_X, ALU.max)\
                        .then_inc(reduced, 1)

                def negate(kind, b):
                    u = unit_no(kind, b)
                    dve.wait_ge(desk_full, desk_use("m" + kind, b) + 1)
                    nc.vector.tensor_scalar(ng[:], desk[0:TILES, 0:P], -1.0, None, ALU.mult).then_inc(desk_free, 1)
                    dve.wait_ge(desk_free, desk_use("m" + kind, b) + 1)
                    if before(kind, b):
                        pk, pb = before(kind, b)
                        dve.wait_ge(rows_in[pk], 16 * NPART * (pb + 1))
                    nc.vector.tensor_copy(ng_p[:, 0, :], ng[:]).then_inc(neg_step, 1)
                    dve.wait_ge(neg_step, 5 * u + 1)
                    nc.vector.tensor_tensor(ng_r[:], ng[:], ng_p[:, 0, :], ALU.subtract).then_inc(neg_step, 1)
                    dve.wait_ge(neg_step, 5 * u + 2)
                    nc.vector.tensor_copy(ng_p[:, 1, :], ng_r[:]).then_inc(neg_step, 1)
                    dve.wait_ge(neg_step, 5 * u + 3)
                    nc.vector.tensor_tensor(ng_p[:, 2, :], ng_r[:], ng_p[:, 1, :], ALU.subtract).then_inc(neg_step, 2)

                def values(kind, b):
                    if not exists(b):
                        return
                    dve.wait_ge(desk_full, desk_use("v" + kind, b) + 1)
                    if not isinstance(b, int) or b >= 1:
                        dve.wait_ge(summed, 8 * (unit_no(kind, b - 1) + 1))
                    for g in range(GQ):
                        last = nc.vector.tensor_tensor(
                            va[kind][:, :, g, :, HD * g:HD * g + HD],
                            desk.rearrange("p (n g j d) -> p n g j d", n=NB, g=GQ, j=4)[:, :, g],
                            w_in[kind][:, W_BV + 64 * g:W_BV + 64 * g + 64].rearrange("p (j d) -> p j d", j=4)
                            .unsqueeze(1).broadcast_to([P, NB, 4, HD]), ALU.add)
                        if g == 0:
                            last.then_inc(v_ready[kind], 1)
                        else:
                            last.then_inc(desk_free, 1)

                def merge(kind, b):
                    u = unit_no(kind, b)
                    dve.wait_ge(summed, 8 * u + 8)
                    dve.wait_ge(low_out, u + 1)
                    at_least(dve, o_ready, u)
                    nc.vector.scalar_tensor_tensor(out=u_all[:], in0=sums, scalar=high[:], in1=u_low[:],
                                                   op0=ALU.mult, op1=ALU.add)
                    nc.vector.scalar_tensor_tensor(out=s_all[:], in0=sums, scalar=low[:], in1=s_low[:],
                                                   op0=ALU.mult, op1=ALU.add).then_inc(high_out, 1)
                    dve.wait_ge(high_out, u + 1)
                    settle(nc, scrap)
                    nc.vector.stream_shuffle(s_right[:], s_all[:], mask=list(range(HD, 32)) + list(range(HD)))\
                        .then_inc(swapped, 1)

                def slot_program(i, slot):
                    (kn, bn), (ka, ba), (kb, bb), (ko, bo) = units(i, slot)
                    for n in range(TILES):
                        if exists(ba):
                            reduce(ka, ba, n)
                        if n == 1 and exists(bb):
                            negate(kb, bb)
                        if n == 10:
                            values(kn, bn)
                        if exists(bo):
                            if n == 12:
                                merge(ko, bo)
                            if n == 26 and ko == "T":
                                at = desk_use("oT", bo)
                                dve.wait_ge(desk_full, at + 1)
                                dve.wait_ge(affine_done, input_no("xres", bo) + 1)
                                if not isinstance(bo, int) or bo >= 1:
                                    dve.wait_ge(desk_full, desk_use("vC", bo - 1) + 1)
                                nc.vector.scalar_tensor_tensor(out=t_outT[:], in0=desk, scalar=w_out["T"][:, O_B:O_B + 1],
                                                               in1=xres[:], op0=ALU.add, op1=ALU.add)\
                                    .then_inc(desk_free, 1)
                            if n == 26 and ko == "C":
                                dve.wait_ge(desk_full, desk_use("oC", bo) + 1)
                                dve.wait_ge(x_biased, bo + 1)
                                xb = X[:, bass.ds(NB * bo, NB), 0:P]
                                nc.vector.tensor_tensor(xb, xb, desk.rearrange("p (n d) -> p n d", n=NB), ALU.add)\
                                    .then_inc(desk_free, 1)

                values("S", 0)
                whole_loop(dve, slot_program)

            @block.scalar
            def _(act):
                def project(kind, b, c):
                    if not exists(b):
                        return
                    n = 2 * unit_no(kind, b) + c
                    act.wait_ge(desk_full, desk_use("qk"[c] + kind, b) + 1)
                    at_least(act, rem_done, n - 1)
                    nc.scalar.activation(f32[c][:], desk, ACT.Identity, bias=w_in[kind][:, W_BQ + c:W_BQ + c + 1])\
                        .then_inc(desk_free, 1)
                    act.wait_ge(desk_free, desk_use("qk"[c] + kind, b) + 1)
                    if before(kind, b):
                        pk, pb = before(kind, b)
                        act.wait_ge(stack_in[pk], 16 * 2 * NPROD * (pb + 1))
                    nc.scalar.activation(parts[c][:, 0, :], f32[c][:], ACT.Copy).then_inc(hi_done, 1)

                def middle(kind, b, c):
                    if not exists(b):
                        return
                    act.wait_ge(rem_done, 2 * unit_no(kind, b) + c + 1)
                    nc.scalar.activation(parts[c][:, 1, :], rem[c][:], ACT.Copy).then_inc(mid_done, 1)

                def exponential(kind, b, n):
                    u = unit_no(kind, b)
                    t0 = first_key(kind, n)
                    act.wait_ge(logits_in, TILES * u + n + 1)
                    if n % 4 == 0:
                        at_least(act, summed, 8 * u + n // 4 - 1)
                    nc.scalar.activation(probs[:, n // 4 % 2, n % 4, t0:T], psum[:, LOGITS + ring_place(kind, b, n, RC), t0:T], ACT.Exp,
                                         scale=SCALE).then_inc(exped, 1)

                def reciprocal(kind, b):
                    u = unit_no(kind, b)
                    act.wait_ge(swapped, u + 1)
                    nc.scalar.activation(s_log[:], s_right[:], ACT.Ln).then_inc(logged, 1)
                    act.wait_ge(logged, u + 1)
                    at_least(act, o_ready, u)
                    nc.scalar.activation(s_recip[:], s_log[:], ACT.Exp, scale=-1.0).then_inc(recip, 1)

                def slot_program(i, slot):
                    (kn, bn), _, (kb, bb), (ko, bo) = units(i, slot)
                    for n in range(TILES):
                        if n == 16 and exists(bo):
                            reciprocal(ko, bo)
                        if n == 4:
                            project(kn, bn, 0)
                        if n == 7:
                            project(kn, bn, 1)
                        if n == 9:
                            middle(kn, bn, 0)
                        if n == 12:
                            middle(kn, bn, 1)
                        if n == 28 and exists(bb):
                            u = unit_no(kb, bb)
                            act.wait_ge(summed, 8 * u + 4)
                            at_least(act, high_out, u)
                            nc.scalar.activation(u_low[:], sums, ACT.Copy, scale=low[:])
                            nc.scalar.activation(s_low[:], sums, ACT.Copy, scale=high[:]).then_inc(low_out, 1)
                        if n == 26 and ko == "S" and exists(bo):
                            act.wait_ge(desk_full, desk_use("oS", bo) + 1)
                            if not isinstance(bo, int) or bo >= 1:
                                act.wait_ge(desk_full, desk_use("qC", bo - 1) + 1)
                            nc.scalar.activation(s_outT[:], desk, ACT.Identity, bias=w_out["S"][:, O_B:O_B + 1])\
                                .then_inc(desk_free, 1)
                        if n < LAG and exists(bo):
                            exponential(ko, bo, TILES - LAG + n)
                        if n >= LAG and exists(bb):
                            exponential(kb, bb, n - LAG)

                nc.scalar.add_instruction(mybir.InstLoadActFuncSet(
                    name=nc.get_next_instruction_name(), engine=mybir.EngineType.Activation, ins=[], outs=[],
                    act_func_set_id=EXP_AND_LN))
                project("S", 0, 0)
                project("S", 0, 1)
                middle("S", 0, 0)
                middle("S", 0, 1)
                whole_loop(act, slot_program)

            @block.tensor
            def _(pe):
                pe.wait_ge(ones_in, 1)
                pe.wait_ge(consts, 3)
                pe.wait_ge(w_fixed, 48)

                def project(kind, b, c):
                    if not exists(b):
                        return
                    source = {"S": xn, "T": xt, "C": t_outT if c else s_outT}[kind]
                    use = desk_use("qkv"[c] + kind, b)
                    at_least(pe, desk_free, use)
                    if kind == "C":
                        s_use, t_use = desk_use("oS", b) + 1, desk_use("oT", b) + 1
                        pe.wait_ge(desk_free, t_use if c else s_use)
                    elif c == 0:
                        pe.wait_ge(win_in[kind], 16 * b + 16)
                        pe.wait_ge(affine_done, input_no({"S": "xn", "T": "xt"}[kind], b) + 1)
                    if c < 2:
                        nc.tensor.matmul(desk, w_in[kind][:, P * c:P * c + P], source[:], start=True, stop=True)\
                            .then_inc(desk_full, 1)
                    else:
                        for n in range(NB):
                            last = nc.tensor.matmul(desk[:, P * n:P * n + P], source[:, P * n:P * n + P],
                                                    w_in[kind][:, W_V:W_V + P], start=True, stop=True)
                        last.then_inc(desk_full, 1)

                def score(kind, b, n):
                    u = unit_no(kind, b)
                    if n == 0:
                        pe.wait_ge(stack_in[kind], 16 * 2 * NPROD * (b + 1))
                    at_least(pe, reduced, TILES * u + n - RL + 1)
                    hd, tb = n // NB, n % NB
                    keys = P * (tb + 1) if kind == "T" else T
                    last = nc.tensor.matmul(psum[:, ring_place(kind, b, n, RL), 0:keys], qs[kind][0:RA, hd, P * tb:P * tb + P],
                                            ks[kind][0:RA, hd, 0:keys], start=True, stop=True)
                    if kind == "T":
                        last = nc.tensor.matmul(psum[:, ring_place(kind, b, n, RL), P * tb:keys], ident_bf[:], mask_row[:],
                                                start=False, stop=True, skip_group_check=True)
                    last.then_inc(scored, 1)

                def logits(kind, b, n):
                    u = unit_no(kind, b)
                    if n == 0:
                        pe.wait_ge(rows_in[kind], 16 * NPART * (b + 1))
                    at_least(pe, exped, TILES * u + n - RC + 1)
                    hd, s, t0 = n // 16 * 4 + n % 4, n // 4 % NB, first_key(kind, n)
                    bank = LOGITS + ring_place(kind, b, n, RC)
                    last = nc.tensor.matmul(psum[:, bank, t0:T], ks[kind][0:RB, hd, P * s:P * s + P],
                                            qs[kind][0:RB, hd, t0:T], start=True, stop=True)
                    if kind == "T":
                        last = nc.tensor.matmul(psum[:, bank, t0:t0 + P], ident_bf[:], mask_col[:],
                                                start=False, stop=True, skip_group_check=True)
                    last.then_inc(logits_in, 1)

                def weigh(kind, b, q):
                    u = unit_no(kind, b)
                    g, s = q // NB, q % NB
                    pe.wait_ge(exped, TILES * u + 4 * q + 4)
                    if q == 0:
                        pe.wait_ge(v_ready[kind], b + 1)
                        pe.wait_ge(desk_free, desk_use("v" + kind, b) + 1)
                        at_least(pe, high_out, u)
                    if q == NB:
                        pe.wait_ge(low_out, u + 1)
                    t0 = first_key(kind, 4 * q)
                    for j in range(4):
                        last = nc.tensor.matmul(sums[32 * j:32 * j + 32, t0:T], va[kind][:, s, g, j, :],
                                                probs[:, q % 2, j, t0:T], start=(s == 0),
                                                stop=(kind == "T" or s == NB - 1), skip_group_check=(kind == "T"))
                    last.then_inc(summed, 1)

                def output(kind, b):
                    u = unit_no(kind, b)
                    use = desk_use("o" + kind, b)
                    pe.wait_ge(o_ready, u + 1)
                    pe.wait_ge(desk_free, use)
                    if kind == "C":
                        for n in range(NB):
                            last = nc.tensor.matmul(desk[:, P * n:P * n + P], oT[:, P * n:P * n + P],
                                                    w_out[kind][:, O_W:O_W + P], start=True, stop=True)
                    else:
                        pe.wait_ge(wout_in[kind], 16 * b + 16)
                        last = nc.tensor.matmul(desk, w_out[kind][:, O_W:O_W + P], oT[:], start=True, stop=True)
                    last.then_inc(desk_full, 1)

                def slot_program(i, slot):
                    (kn, bn), (ka, ba), (kb, bb), (ko, bo) = units(i, slot)
                    for n in range(TILES):
                        if exists(ba):
                            score(ka, ba, n)
                        if n == 1 and exists(bb):
                            pe.wait_ge(reduced, TILES * (unit_no(kb, bb) + 1))
                            at_least(pe, desk_free, desk_use("m" + kb, bb))
                            nc.tensor.transpose(desk[0:TILES, 0:P], mx[kb][:], ident[:]).then_inc(desk_full, 1)
                        if n in (4, 7, 10):
                            project(kn, bn, (n - 4) // 3)
                        if n < LAG and exists(bo):
                            logits(ko, bo, TILES - LAG + n)
                        if n >= LAG and exists(bb):
                            logits(kb, bb, n - LAG)
                        if n % 4 == 3:
                            q = (n - LAG) // 4 - 1
                            if q < 0 and exists(bo):
                                weigh(ko, bo, q + 8)
                            if q >= 0 and exists(bb):
                                weigh(kb, bb, q)
                        if n == 26 and exists(bo):
                            output(ko, bo)

                for c in range(3):
                    project("S", 0, c)
                whole_loop(pe, slot_program)


def feed_forward(nc, shared, mlp_w1, mlp_b1, mlp_w2, mlp_b2, out_v):
    scrap, ident, low, high, eps_t, minus_half, norm_cols, expert, X, xhatT, psum = shared
    with ExitStack() as ctx:
        def sb(name, shape, dt=F32):
            return ctx.enter_context(nc.sbuf_tensor(name, shape, dt))

        def sem(name):
            return ctx.enter_context(nc.semaphore(name))

        w1 = sb("w1", [P, F])
        b1 = sb("b1", [P, F // P])
        w2 = sb("w2", [P, F // P, P])
        b2 = sb("b2", [P, P])
        six = sb("six3", [P, NB, 6])
        mv = sb("mv3", [P, NB, 2])
        vare = sb("vare3", [P, NB])
        rstd = sb("rstd3_t", [P, NB])
        xs = sb("xs3", [P, NB, P])
        hT = sb("hT", [P, T])
        gT = sb("gT", [P, F // P, T])
        h2 = sb("h2", [P, 2, NB, P])
        base = sb("base", [P, NB, P])
        y = sb("y", [P, 2, NB, P])

        loaded = sem("loaded3")
        h2_in = [sem("h2_in0"), sem("h2_in1")]
        six_r, stats, var, root = sem("six_r"), sem("stats_r"), sem("var_r"), sem("root_r")
        normed, turned, hT_ready = sem("normed_r"), sem("turned_r"), sem("hT_ready")
        up_done, gelu_done, down_done = sem("up_done"), sem("gelu_done"), sem("down_done")
        base_a, base_b = sem("base_a"), sem("base_b")
        y_ready = sem("y_ready")
        stored = [sem("stored0"), sem("stored1")]
        TURN, DOWN = 0, 5

        with nc.Block() as block:
            @block.sync
            def _(sp):
                for tile, source in ((w1, mlp_w1), (b1, mlp_b1), (w2, mlp_w2), (b2, mlp_b2)):
                    sp.dma_start(tile[:], source).then_inc(loaded, 16)

                def fetch(b, odd):
                    sp.dma_start(h2[:, odd, :, :], out_v[bass.ds(b, 1), :, :, :].rearrange("b p n d -> p (b n) d"))\
                        .then_inc(h2_in[odd], 16)

                fetch(0, 0)
                fetch(1, 1)

                def store(b, odd):
                    sp.wait_ge(y_ready, b + 1)
                    sp.dma_start(out_v[bass.ds(b, 1), :, :, :].rearrange("b p n d -> p (b n) d"), y[:, odd, :, :])\
                        .then_inc(stored[odd], 16)

                with sp.Fori(0, B // 2 - 1) as pair:
                    for odd in range(2):
                        b = 2 * pair + odd
                        sp.wait_ge(base_a, b + 1)
                        fetch(b + 2, odd)
                        store(b, odd)
                for odd in range(2):
                    store(B - 2 + odd, odd)
                sp.wait_ge(stored[0], 8 * B)
                sp.wait_ge(stored[1], 8 * B)

            @block.gpsimd
            def _(pool):
                pool.wait_ge(loaded, 64)

                def sequence(b, odd, pair):
                    pool.wait_ge(stats, b + 1)
                    nc.gpsimd.tensor_tensor(vare[:], mv[:, :, 1], eps_t[:], ALU.add).then_inc(var, 1)
                    pool.wait_ge(var, b + 1)
                    nc.gpsimd.tensor_tensor(rstd[:], vare[:], minus_half[:], ALU.pow).then_inc(root, 1)
                    pool.wait_ge(h2_in[odd], 16 * pair + 16)
                    at_least(pool, y_ready, b)
                    nc.gpsimd.tensor_tensor(base[:], h2[:, odd, :, :], X[:, bass.ds(NB * b, NB), 0:P], ALU.add)\
                        .then_inc(base_a, 1)
                    pool.wait_ge(base_a, b + 1)
                    nc.gpsimd.tensor_tensor(base[:], base[:], b2[:].unsqueeze(1).broadcast_to([P, NB, P]), ALU.add)\
                        .then_inc(base_b, 1)

                for odd in range(2):
                    sequence(odd, odd, 0)
                with pool.Fori(1, B // 2) as pair:
                    for odd in range(2):
                        sequence(2 * pair + odd, odd, pair)

            @block.vector
            def _(dve):
                def normalise(b):
                    for n in range(NB):
                        last = nc.vector.bn_stats(six[:, n, :], tokens(X, b, n))
                    last.then_inc(six_r, 1)
                    dve.wait_ge(six_r, b + 1)
                    settle(nc, scrap)
                    for n in range(NB):
                        last = nc.vector.bn_aggr(mv[:, n, :], six[:, n, :])
                    last.then_inc(stats, 1)
                    dve.wait_ge(stats, b + 1)
                    dve.wait_ge(root, b + 1)
                    at_least(dve, turned, b)
                    for n in range(NB):
                        last = nc.vector.tensor_scalar(xs[:, n, :], tokens(X, b, n), mv[:, n, 0:1], rstd[:, n:n + 1],
                                                       ALU.subtract, ALU.mult)
                    last.then_inc(normed, 1)

                def finish(b, odd, pair):
                    dve.wait_ge(down_done, b + 1)
                    dve.wait_ge(base_b, b + 1)
                    at_least(dve, stored[odd], 16 * pair)
                    nc.vector.tensor_tensor(y[:, odd, :, :], base[:], psum[:, DOWN, :]
                                            .rearrange("p (n d) -> p n d", n=NB), ALU.add).then_inc(y_ready, 1)

                def scale_shift(b):
                    dve.wait_ge(turned, b + 1)
                    at_least(dve, up_done, b)
                    nc.vector.tensor_scalar(hT[:], psum[:, TURN, :], norm_cols[:, 4:5], norm_cols[:, 5:6],
                                            ALU.mult, ALU.add).then_inc(hT_ready, 1)

                def pass_of(pair, odd):
                    normalise(2 * pair + odd + 1)
                    scale_shift(2 * pair + odd + 1)
                    finish(2 * pair + odd, odd, pair)

                normalise(0)
                scale_shift(0)
                pass_of(0, 0)
                pass_of(0, 1)
                with dve.Fori(1, B // 2 - 1) as pair:
                    pass_of(pair, 0)
                    pass_of(pair, 1)
                pass_of(B // 2 - 1, 0)
                finish(B - 1, 1, B // 2 - 1)

            @block.scalar
            def _(act):
                act.wait_ge(loaded, 64)

                def gelu(b):
                    act.wait_ge(up_done, b + 1)
                    at_least(act, down_done, b)
                    for f in range(F // P):
                        last = nc.scalar.activation(gT[:, f, :], psum[:, 1 + f, :], ACT.Gelu, bias=b1[:, f:f + 1])
                    last.then_inc(gelu_done, 1)

                gelu(0)
                with act.Fori(1, B) as b:
                    gelu(b)

            @block.tensor
            def _(pe):
                pe.wait_ge(loaded, 64)

                def turn(b):
                    pe.wait_ge(normed, b + 1)
                    at_least(pe, hT_ready, b)
                    for n in range(NB):
                        last = nc.tensor.transpose(psum[:, TURN, P * n:P * n + P], xs[:, n, :], ident[:])
                    last.then_inc(turned, 1)

                def up(b):
                    pe.wait_ge(hT_ready, b + 1)
                    at_least(pe, gelu_done, b)
                    for f in range(F // P):
                        last = nc.tensor.matmul(psum[:, 1 + f, :], w1[:, P * f:P * f + P], hT[:], start=True, stop=True)
                    last.then_inc(up_done, 1)

                def down(b):
                    pe.wait_ge(gelu_done, b + 1)
                    at_least(pe, y_ready, b)
                    for n in range(NB):
                        for f in range(F // P):
                            last = nc.tensor.matmul(psum[:, DOWN, P * n:P * n + P], gT[:, f, P * n:P * n + P],
                                                    w2[:, f, :], start=(f == 0), stop=(f == F // P - 1))
                    last.then_inc(down_done, 1)

                turn(0)
                up(0)
                turn(1)
                down(0)
                with pe.Fori(1, B - 1) as b:
                    up(b)
                    turn(b + 1)
                    down(b)
                up(B - 1)
                down(B - 1)


def kernel(**inputs):
    import numpy as np
    from concourse import bacc
    from concourse.bass_utils import run_bass_kernel_spmd

    a = {k.removeprefix("L0_").removeprefix("ffn_"): np.asarray(v) for k, v in inputs.items()}
    rows = np.arange(P).reshape(GQ, 4, HD).transpose(1, 0, 2).reshape(P)
    mixed = np.arange(P).reshape(H, HD).T.reshape(P)

    def columns(*parts):
        return np.concatenate([p if p.ndim == 2 else p[:, None] for p in parts], axis=1)

    def spread(row):
        return np.broadcast_to(row, (P, P))

    def pack_in(wq, wk, wv, bq, bk, bv):
        return columns(wq[mixed].T, wk[mixed].T, wv.T, bq[mixed], bk[mixed], spread(bv))

    def thirds(w):
        return w[0:P], w[P:2 * P], w[2 * P:3 * P]

    w12 = np.zeros((P, 64), np.float32)
    w12[:, 0:10] = a["attn_W1"]
    w12[:, 32:42] = a["attn_W2"].T
    given = {
        "x_ids": np.asarray(a["x"]).reshape(B * NB, P).T,
        "table": a["tok_W"].T,
        "w12": w12,
        "router_w1": a["router_w1"].T,
        "router_b1": a["router_b1"][:, None],
        "router_w2": a["router_w2"].T,
        "router_b2": np.broadcast_to(a["router_b2"], (B, 2 * K)),
        "norms": columns(a["norm_s_w"], a["norm_s_b"], a["norm_t_w"], a["norm_t_b"], a["norm_mlp_w"], a["norm_mlp_b"]),
        "s_in": np.stack([pack_in(*thirds(a["sp_in_w"][k]), *thirds(a["sp_in_b"][k])) for k in range(K)]),
        "s_out": np.stack([columns(a["sp_out_w"][k].T[rows], a["sp_out_b"][k]) for k in range(K)]),
        "t_in": np.stack([pack_in(a["tq_w"][k], a["tk_w"][k], a["tv_w"][k], a["tq_b"][k], a["tk_b"][k], a["tv_b"][k])
                          for k in range(K)]),
        "t_out": np.stack([columns(a["tp_w"][k].T[rows], a["tp_b"][k]) for k in range(K)]),
        "c_in": pack_in(*thirds(a["cross_in_w"]), *thirds(a["cross_in_b"])),
        "c_out": columns(a["cross_out_w"].T[rows], a["cross_out_b"]),
        "c_bias": spread(a["cross_out_b"]),
        "mlp_w1": a["mlp_w1"].T,
        "mlp_b1": a["mlp_b1"].reshape(F // P, P).T,
        "mlp_w2": a["mlp_w2"].T.reshape(F // P, P, P).transpose(1, 0, 2),
        "mlp_b2": spread(a["mlp_b2"]),
    }
    nc = bacc.Bacc("TRN2", target_bir_lowering=False, num_devices=1)
    arrays, args = {}, []
    for name, value in given.items():
        arrays[f"in_{name}"] = np.ascontiguousarray(value)
        args.append(nc.dram_tensor(f"in_{name}", value.shape, mybir.dt.from_np(value.dtype), kind="ExternalInput").ap())
    args.append(nc.dram_tensor("out_0", (B, T, P), F32, kind="ExternalOutput").ap())
    program(nc, *args)
    r = run_bass_kernel_spmd(nc, [arrays], core_ids=[0])
    return r.results[0]["out_0"]
```
